# Optimizing a Trainium2 kernel written in Bass

```python
import numpy as np
import jax
import jax.numpy as jnp

def _softmax(x, axis=-1):
    return jax.nn.softmax(x, axis=axis)
def _gelu(x):
    return jax.nn.gelu(x, approximate=True)
def _silu(x):
    return jax.nn.silu(x)
def _sigmoid(x):
    return jax.nn.sigmoid(x)
def _layernorm(x, axis=-1, eps=1e-5):
    m = jnp.mean(x, axis=axis, keepdims=True)
    v = jnp.var(x, axis=axis, keepdims=True)
    return (x - m) / jnp.sqrt(v + eps)
def _scatter_add(tgt, idx, src, axis=0):
    return tgt.at[idx].add(src)
def _segment_sum(src, seg, n):
    return jax.ops.segment_sum(src, seg, n)

kernel_name = 'mk_conv_seq_d1_conv_nchw1024_6e6e71'

def setup_inputs(seed: int = 0):
    np.random.seed(seed)
    _w = jnp.asarray
    def _rec_inputs():
        import jax
        import jax.numpy as jnp
        _gk = jax.random.key(seed)
        x = -0.000125 + 0.9999 * jax.random.normal(jax.random.fold_in(_gk, 1), (32, 1024, 32, 32), jnp.float32)
        return x
    x = _rec_inputs()
    def _L0_conv_setup():
        import jax, jax.numpy as jnp
        import numpy as np
        HPLANES = 256

        def _maxpool2(x):
            B, C, H, W = x.shape
            return x.reshape(B, C, H // 2, 2, W // 2, 2).max(axis=(3, 5))
        key = jax.random.key(seed)
        ks = jax.random.split(key, 5)
        B, C, H, W = (32, 1024, 32, 32)
        hp = HPLANES
        std = 0.01
        return {'x': jax.random.normal(ks[0], (B, C, H, W), jnp.float32), 'theta_w': jax.random.normal(ks[1], (hp, C), jnp.float32) * std, 'theta_b': jnp.zeros((hp,), jnp.float32), 'phi_w': jax.random.normal(ks[2], (hp, C), jnp.float32) * std, 'phi_b': jnp.zeros((hp,), jnp.float32), 'g_w': jax.random.normal(ks[3], (hp, C), jnp.float32) * std, 'g_b': jnp.zeros((hp,), jnp.float32), 'z_w': jax.random.normal(ks[4], (C, hp), jnp.float32) * std, 'z_b': jnp.zeros((C,), jnp.float32)}
    _L0_conv_all = _L0_conv_setup()
    _L0_conv_in = {k: v for k, v in _L0_conv_all.items() if k in ('theta_w', 'theta_b', 'phi_w', 'phi_b', 'g_w', 'g_b', 'z_w', 'z_b', )}
    del _L0_conv_all

    return {
        "x": x,
        "L0_conv_theta_w": _L0_conv_in["theta_w"],
        "L0_conv_theta_b": _L0_conv_in["theta_b"],
        "L0_conv_phi_w": _L0_conv_in["phi_w"],
        "L0_conv_phi_b": _L0_conv_in["phi_b"],
        "L0_conv_g_w": _L0_conv_in["g_w"],
        "L0_conv_g_b": _L0_conv_in["g_b"],
        "L0_conv_z_w": _L0_conv_in["z_w"],
        "L0_conv_z_b": _L0_conv_in["z_b"],
    }

def reference(x, L0_conv_theta_w, L0_conv_theta_b, L0_conv_phi_w, L0_conv_phi_b, L0_conv_g_w, L0_conv_g_b, L0_conv_z_w, L0_conv_z_b):
    import jax
    import jax.numpy as jnp
    def _L0_conv_ref(x, theta_w, theta_b, phi_w, phi_b, g_w, g_b, z_w, z_b):
        import jax, jax.numpy as jnp
        import numpy as np
        HPLANES = 256

        def _maxpool2(x):
            B, C, H, W = x.shape
            return x.reshape(B, C, H // 2, 2, W // 2, 2).max(axis=(3, 5))
        B, C, H, W = x.shape
        hp = theta_w.shape[0]
        q = jnp.einsum('bchw,dc->bdhw', x, theta_w) + theta_b[None, :, None, None]
        q = q.reshape(B, hp, H * W)
        xpool = _maxpool2(x)
        k = jnp.einsum('bchw,dc->bdhw', xpool, phi_w) + phi_b[None, :, None, None]
        k = k.reshape(B, hp, -1)
        v = jnp.einsum('bchw,dc->bdhw', xpool, g_w) + g_b[None, :, None, None]
        v = v.reshape(B, hp, -1)
        qk = jnp.einsum('bdn,bdm->bnm', q, k) * hp ** (-0.5)
        p = jax.nn.softmax(qk, axis=-1)
        vp = jnp.einsum('bdm,bnm->bdn', v, p)
        vp = vp.reshape(B, hp, H, W)
        out = jnp.einsum('bdhw,cd->bchw', vp, z_w) + z_b[None, :, None, None]
        return out + x

    def _gn(v, G=32, eps=1e-5):
        B_, C_, H_, W_ = v.shape
        g = v.reshape(B_, G, C_ // G, H_, W_)
        m = jnp.mean(g, axis=(2, 3, 4), keepdims=True)
        s = jnp.var(g, axis=(2, 3, 4), keepdims=True)
        return ((g - m) / jnp.sqrt(s + eps)).reshape(v.shape)

    def _ln_c(v, eps=1e-6):
        m = jnp.mean(v, axis=1, keepdims=True)
        s = jnp.var(v, axis=1, keepdims=True)
        return (v - m) / jnp.sqrt(s + eps)

    def _ln_t(v, eps=1e-5):
        m = jnp.mean(v, axis=-1, keepdims=True)
        s = jnp.var(v, axis=-1, keepdims=True)
        return (v - m) / jnp.sqrt(s + eps)

    def _to_tokens(v):
        B_, C_, H_, W_ = v.shape
        return v.reshape(B_, C_, H_ * W_).transpose(0, 2, 1)
    def _from_tokens(t, like):
        B_, C_, H_, W_ = like.shape
        return t.transpose(0, 2, 1).reshape(B_, C_, H_, W_)

    x = _L0_conv_ref(x, L0_conv_theta_w, L0_conv_theta_b, L0_conv_phi_w, L0_conv_phi_b, L0_conv_g_w, L0_conv_g_b, L0_conv_z_w, L0_conv_z_b)
    return x


_drawn_inputs = setup_inputs


def setup_inputs(seed=0):
    import zlib

    import numpy as np

    out = dict(_drawn_inputs(seed))
    spreads = {'L0_conv_theta_b': (0.0, 0.8),
     'L0_conv_phi_b': (0.0, 0.8),
     'L0_conv_g_b': (0.0, 0.467),
     'L0_conv_z_b': (0.0, 0.1)}
    factors = {'L0_conv_theta_w': 8.0, 'L0_conv_phi_w': 8.0}
    for name, (base, spread) in spreads.items():
        noise = np.random.default_rng([zlib.crc32(name.encode()), seed]).standard_normal(out[name].shape)
        drawn = base * np.exp(spread * noise) if base else spread * noise
        out[name] = jnp.asarray(drawn.astype(out[name].dtype))
    for name, factor in factors.items():
        out[name] = (out[name] * factor).astype(out[name].dtype)
    return out
```

```python
import concourse.bass as bass
from concourse import mybir
from contextlib import ExitStack

P = 128
IMAGES = 32
C = 1024
D = 256
SIDE = 32
N = SIDE * SIDE
M = N // 4
KT = C // P
DT = D // P
MT = M // P
H = N // 2
MH = M // 2
NT = H // P
HALVES = 2 * IMAGES
BUFS = 4
TURNS = HALVES // BUFS
CH = 4
KC = KT // CH
SCALE = float(D) ** -0.5
STORES = 4
OS = KT // STORES
LOADS = 2
TH_B, PH_B, G_B, Z_B = 0, DT, 2 * DT, 3 * DT
NB = 3 * DT + KT


def non_local_block(nc, x, theta_wt, phi_wt, g_wt, z_wt, biases, out):
    f32 = mybir.dt.float32
    f32r = mybir.dt.float32r
    ALU = mybir.AluOpType
    ACT = mybir.ActivationFunctionType
    AX = mybir.AxisListType

    x_v = x.rearrange("(u i) (k p) (j n) -> i j u p k n", i=BUFS // 2, p=P, j=2)
    out_v = out.rearrange("b (k p) (j n) -> b j p k n", p=P, j=2)
    weights_dram = [theta_wt.rearrange("(k p) d -> p k d", p=P), phi_wt.rearrange("(k p) d -> p k d", p=P),
                    g_wt.rearrange("(k p) d -> p k d", p=P), z_wt.rearrange("(t p) c -> p t c", p=P)]

    with ExitStack() as ctx:
        def sb(name, shape, dt):
            return ctx.enter_context(nc.sbuf_tensor(name, shape, dt))

        def sem(name):
            return ctx.enter_context(nc.semaphore(name))

        theta = [sb(f"theta_{s}", [P, KT, D], f32r) for s in ("hi", "lo")]
        phi = [sb(f"phi_{s}", [P, KT, D], f32r) for s in ("hi", "lo")]
        gw = [sb(f"g_{s}", [P, KT, D], f32r) for s in ("hi", "lo")]
        zw = [sb(f"z_{s}", [P, DT, C], f32r) for s in ("hi", "lo")]
        weights = [theta, phi, gw, zw]
        bias = sb("bias", [P, NB], f32)
        phi_bias = sb("phi_bias", [P, DT], f32)
        ident = sb("ident", [P, P], f32)
        xb = [sb(f"x{i}", [P, KT, H], f32) for i in range(BUFS)]
        xs = [sb(f"x_split_{s}", [P, KT, H], f32r) for s in ("hi", "lo")]
        rowmax = sb("rowmax", [P, 2, KC * H // 2], f32)
        pooled = sb("pooled", [P, KT, MH], f32)
        xp = [sb(f"xp_{s}", [P, KT, M], f32r) for s in ("hi", "lo")]
        q = [sb(f"q_{s}", [P, DT, H], f32r) for s in ("hi", "lo")]
        k = [sb(f"k_{s}", [P, DT, M], f32r) for s in ("hi", "lo")]
        vt = [sb(f"vt_{s}", [P, MT, D], f32r) for s in ("hi", "lo")]
        probs = sb("probs", [P, NT, M], f32)
        negmax = sb("negmax", [P, NT], f32)
        rowsum = sb("rowsum", [P, NT], f32)
        rowinv = sb("rowinv", [P, NT], f32)
        pt = [sb(f"pt_{s}", [P, MT, H], f32r) for s in ("hi", "lo")]
        att = [sb(f"att_{s}", [P, DT, H], f32r) for s in ("hi", "lo")]

        bank = [ctx.enter_context(nc.psum_tensor(f"bank{i}", [P, 512], f32)) for i in range(8)]
        q_bank = bank[0:2]
        s_bank = bank[2:4]
        a_bank = bank[2:4]
        t_bank = bank[4:6]
        k_bank, v_bank = bank[4], bank[5]
        o_bank = [bank[6], bank[7], bank[4], bank[5]]

        w_loaded = [sem(f"w_loaded{i}") for i in range(4)]
        bias_loaded = sem("bias_loaded")
        w_hi = sem("w_hi")
        w_ready = sem("w_ready")
        phi_bias_ready = sem("phi_bias_ready")
        ident_zero = sem("ident_zero")
        ident_ready = sem("ident_ready")
        x_loaded = [sem(f"x_loaded{i}") for i in range(BUFS)]
        stored = sem("stored")
        x_hi = sem("x_hi")
        x_ready = sem("x_ready")
        x_used = sem("x_used")
        rowmax_done = sem("rowmax_done")
        pooled_done = sem("pooled_done")
        xp_ready = sem("xp_ready")
        q_done = sem("q_done")
        q_hi = sem("q_hi")
        q_ready = sem("q_ready")
        k_done = sem("k_done")
        k_hi = sem("k_hi")
        k_ready = sem("k_ready")
        v_done = sem("v_done")
        v_hi = sem("v_hi")
        v_ready = sem("v_ready")
        s_done = sem("s_done")
        max_ready = sem("max_ready")
        exp_done = sem("exp_done")
        inv_done = sem("inv_done")
        p_ready = sem("p_ready")
        t_done = sem("t_done")
        pt_hi = sem("pt_hi")
        pt_ready = sem("pt_ready")
        a_done = sem("a_done")
        att_hi = sem("att_hi")
        att_ready = sem("att_ready")
        o_done = sem("o_done")
        o_ready = sem("o_ready")

        HI, LO = 0, 1
        PRODUCTS = ((HI, HI), (HI, LO), (LO, HI))

        THETA, PHI, G, Z = range(4)
        staged = [xb[3][:, 0:4, :].rearrange("p a (b d) -> p (a b) d", d=D),
                  xb[3][:, 4:8, :].rearrange("p a (b d) -> p (a b) d", d=D),
                  xb[2][:, 0:4, :].rearrange("p a (b d) -> p (a b) d", d=D),
                  xb[2][:, 4:8, :].rearrange("p (t a) n -> p t (a n)", t=DT)]

        def raw(t):
            return t.bitcast(f32)

        def flat(t):
            return t[:, :, :].rearrange("p a b -> p (a b)")

        def steps(eng, step):
            with eng.Fori(0, TURNS - 1) as turn:
                for s in range(BUFS):
                    step(turn, s)
            for s in range(BUFS):
                step(TURNS - 1, s)

        def exists(turn, s, ahead):
            return not isinstance(turn, int) or s + ahead < BUFS

        def upto(turn, s, each, more):
            return turn * (BUFS * each) + (s * each + more)

        def image_of(turn, s, more=0):
            return turn * (BUFS // 2) + (s // 2 + more)

        block = ctx.enter_context(nc.Block())

        @block.sync
        def _(sp):
            def load(buf, turn):
                for g in range(LOADS):
                    ks = slice(g * KT // LOADS, (g + 1) * KT // LOADS)
                    sp.dma_start(xb[buf][:, ks, :], x_v[buf // 2, buf % 2, turn, :, ks, :]).then_inc(x_loaded[buf], 16)

            load(0, 0)
            load(1, 0)
            sp.wait_ge(w_ready, len(weights))
            load(2, 0)
            load(3, 0)

            def step(turn, s):
                for g in range(STORES):
                    sp.wait_ge(o_ready, upto(turn, s, KT, (g + 1) * OS))
                    ks = slice(g * OS, (g + 1) * OS)
                    sp.dma_start(out_v[image_of(turn, s), s % 2, :, ks, :], xb[s][:, ks, :]).then_inc(stored, 16)
                if exists(turn, s, BUFS):
                    sp.wait_ge(stored, upto(turn, s, 16 * STORES, 16 * STORES))
                    load(s, turn + 1)

            steps(sp, step)
            sp.wait_ge(stored, HALVES * STORES * 16)

        @block.scalar
        def _(act):
            for i in range(len(weights)):
                act.dma_start(staged[i], weights_dram[i]).then_inc(w_loaded[i], 16)
                if i == 0:
                    act.dma_start(bias[:, :], biases).then_inc(bias_loaded, 16)

            def hi_weights(i):
                act.wait_ge(w_loaded[i], 16)
                nc.scalar.activation(weights[i][HI][:, :, :], staged[i], ACT.Copy,
                                     scale=SCALE if i == PHI else 1.0).then_inc(w_hi, 1)

            def hi_x(buf, c):
                ks = slice(c * KC, (c + 1) * KC)
                nc.scalar.activation(xs[HI][:, ks, :], xb[buf][:, ks, :], ACT.Copy).then_inc(x_hi, 1)

            def hi_q(turn, s):
                for m in range(DT):
                    if m < DT - 1:
                        act.wait_ge(q_done, upto(turn, s, DT - 1, m + 1))
                    else:
                        act.wait_ge(x_used, upto(turn, s, CH, CH))
                    nc.scalar.activation(q[HI][:, m, :], q_bank[m][:, :], ACT.Identity,
                                         bias=bias[:, TH_B + m:TH_B + m + 1]).then_inc(q_hi, 1)

            def hi_kv(image):
                act.wait_ge(k_done, image + 1)
                for m in range(DT):
                    nc.scalar.activation(k[HI][:, m, :], k_bank[:, m * M:(m + 1) * M], ACT.Identity,
                                         bias=phi_bias[:, m:m + 1]).then_inc(k_hi, 1)
                act.wait_ge(v_done, image + 1)
                nc.scalar.activation(flat(vt[HI]), v_bank[:, :], ACT.Copy).then_inc(v_hi, 1)

            hi_weights(THETA)
            act.wait_ge(x_loaded[0], 16 * LOADS)
            for c in range(CH):
                hi_x(0, c)
            for i in (PHI, G, Z):
                hi_weights(i)
            act.wait_ge(x_loaded[1], 16 * LOADS)
            for c in range(CH):
                act.wait_ge(x_used, c + 1)
                hi_x(1, c)
            act.wait_ge(bias_loaded, 16)
            hi_q(0, 0)
            act.wait_ge(phi_bias_ready, 1)
            hi_kv(0)

            def step(turn, s):
                def hi_x_ahead(cs):
                    for c in cs:
                        act.wait_ge(x_used, upto(turn, s, CH, CH + c + 1))
                        hi_x((s + 2) % BUFS, c)

                for i in range(NT):
                    if i % 2 == 0:
                        act.wait_ge(max_ready, upto(turn, s, 2, i // 2 + 1))
                    nc.scalar.activation(probs[:, i, :], s_bank[i // 2][:, (i % 2) * M:(i % 2 + 1) * M], ACT.Exp,
                                         bias=negmax[:, i:i + 1], accum_out=rowsum[:, i:i + 1]).then_inc(exp_done, 1)
                for m in range(MT):
                    act.wait_ge(t_done, upto(turn, s, MT, m + 1))
                    nc.scalar.activation(pt[HI][:, m, :], t_bank[m][:, :], ACT.Copy).then_inc(pt_hi, 1)
                if exists(turn, s, 2):
                    act.wait_ge(x_loaded[(s + 2) % BUFS], turn * (16 * LOADS) + 16 * LOADS * ((s + 2) // BUFS + 1))
                    hi_x_ahead((0, 1))
                for m in range(DT):
                    act.wait_ge(a_done, upto(turn, s, DT, m + 1))
                    nc.scalar.activation(att[HI][:, m, :], a_bank[m][:, :], ACT.Identity,
                                         bias=bias[:, G_B + m:G_B + m + 1]).then_inc(att_hi, 1)
                if exists(turn, s, 1):
                    hi_q(turn, s + 1)
                if exists(turn, s, 2):
                    hi_x_ahead((2, 3))
                if s % 2 and exists(turn, s, 1):
                    hi_kv(image_of(turn, s, 1))

            steps(act, step)

        @block.gpsimd
        def _(pool):
            nc.gpsimd.memset(ident[:, :], 0.0).then_inc(ident_zero, 1)
            pool.wait_ge(ident_zero, 1)
            nc.gpsimd.affine_select(out=ident[:, :], in_=ident[:, :], compare_op=ALU.not_equal, fill=1.0,
                                    base=0, pattern=[[-1, P]], channel_multiplier=1).then_inc(ident_ready, 1)

            def lo_x(turn, s, c, buf):
                ks = slice(c * KC, (c + 1) * KC)
                pool.wait_ge(x_hi, upto(turn, s, CH, c + 1))
                nc.gpsimd.tensor_tensor(xs[LO][:, ks, :], xb[buf][:, ks, :], raw(xs[HI][:, ks, :]),
                                        ALU.subtract).then_inc(x_ready, 1)

            def lo_pooled(turn, s, c):
                ks = slice(c * KC, (c + 1) * KC)
                ms = slice((s % 2) * MH, (s % 2 + 1) * MH)
                pool.wait_ge(pooled_done, upto(turn, s, CH, c + 1))
                nc.gpsimd.tensor_tensor(xp[LO][:, ks, ms], pooled[:, ks, :], raw(xp[HI][:, ks, ms]),
                                        ALU.subtract).then_inc(xp_ready, 1)

            for h in range(2):
                for c in range(CH):
                    lo_pooled(0, h, c)
                    lo_x(0, h, c, h)

            def step(turn, s):
                if exists(turn, s, 2):
                    for c in (0, 1):
                        lo_pooled(turn, s + 2, c)
                    for c in (0, 1):
                        lo_x(turn, s + 2, c, (s + 2) % BUFS)
                    for c in (2, 3):
                        lo_pooled(turn, s + 2, c)
                    for c in (2, 3):
                        lo_x(turn, s + 2, c, (s + 2) % BUFS)

            steps(pool, step)

        @block.vector
        def _(dve):
            def lo_weights(i):
                dve.wait_ge(w_hi, i + 1)
                nc.vector.scalar_tensor_tensor(out=weights[i][LO][:, :, :], in0=staged[i],
                                               scalar=SCALE if i == PHI else 1.0, in1=raw(weights[i][HI][:, :, :]),
                                               op0=ALU.mult, op1=ALU.subtract).then_inc(w_ready, 1)

            def max_pool(turn, s, c, buf):
                ks = slice(c * KC, (c + 1) * KC)
                rows = xb[buf][:, ks, :].rearrange("p k (r two w) -> p (k r) two w", two=2, w=SIDE)
                rm = rowmax[:, c % 2, :]
                nc.vector.tensor_tensor(rm.rearrange("p (r w) -> p r w", w=SIDE), rows[:, :, 0, :], rows[:, :, 1, :],
                                        ALU.max).then_inc(rowmax_done, 1)
                dve.wait_ge(rowmax_done, upto(turn, s, CH, c + 1))
                cols = rm.rearrange("p (w two) -> p w two", two=2)
                nc.vector.tensor_tensor(pooled[:, ks, :].rearrange("p k m -> p (k m)"), cols[:, :, 0], cols[:, :, 1], ALU.max)
                cols = rm.rearrange("p (k w two) -> p k w two", k=KC, two=2)
                nc.vector.tensor_tensor(xp[HI][:, ks, (s % 2) * MH:(s % 2 + 1) * MH], cols[:, :, :, 0], cols[:, :, :, 1],
                                        ALU.max).then_inc(pooled_done, 1)

            def lo_q(turn, s):
                for m in range(DT):
                    dve.wait_ge(q_hi, upto(turn, s, DT, m + 1))
                    nc.vector.scalar_tensor_tensor(out=q[LO][:, m, :], in0=q_bank[m][:, :],
                                                   scalar=bias[:, TH_B + m:TH_B + m + 1], in1=raw(q[HI][:, m, :]),
                                                   op0=ALU.add, op1=ALU.subtract).then_inc(q_ready, 1)

            def lo_kv(image):
                dve.wait_ge(k_hi, image * DT + DT)
                for m in range(DT):
                    nc.vector.scalar_tensor_tensor(out=k[LO][:, m, :], in0=k_bank[:, m * M:(m + 1) * M],
                                                   scalar=phi_bias[:, m:m + 1], in1=raw(k[HI][:, m, :]),
                                                   op0=ALU.add, op1=ALU.subtract).then_inc(k_ready, 1)
                dve.wait_ge(v_hi, image + 1)
                nc.vector.tensor_tensor(flat(vt[LO]), v_bank[:, :], raw(flat(vt[HI])), ALU.subtract).then_inc(v_ready, 1)

            lo_weights(THETA)
            dve.wait_ge(bias_loaded, 16)
            nc.vector.tensor_scalar(phi_bias[:, :], bias[:, PH_B:PH_B + DT], SCALE, None,
                                    ALU.mult).then_inc(phi_bias_ready, 1)
            dve.wait_ge(x_loaded[0], 16 * LOADS)
            for c in range(CH):
                max_pool(0, 0, c, 0)
            for i in (PHI, G, Z):
                lo_weights(i)
            dve.wait_ge(x_loaded[1], 16 * LOADS)
            for c in range(CH):
                dve.wait_ge(xp_ready, c + 1)
                max_pool(0, 1, c, 1)
            lo_q(0, 0)
            dve.wait_ge(phi_bias_ready, 1)
            lo_kv(0)

            def step(turn, s):
                def pool_ahead(cs):
                    for c in cs if exists(turn, s, 2) else ():
                        dve.wait_ge(xp_ready, upto(turn, s + 1, CH, c + 1))
                        max_pool(turn, s + 2, c, (s + 2) % BUFS)

                for b in range(2):
                    dve.wait_ge(s_done, upto(turn, s, 2, b + 1))
                    nc.vector.tensor_reduce(negmax[:, 2 * b:2 * b + 2], s_bank[b][:, :].rearrange("p (i m) -> p i m", m=M),
                                            AX.X, ALU.max, negate=True).then_inc(max_ready, 1)
                if exists(turn, s, 2):
                    dve.wait_ge(x_loaded[(s + 2) % BUFS], turn * (16 * LOADS) + 16 * LOADS * ((s + 2) // BUFS + 1))
                    if s % 2 == 0:
                        dve.wait_ge(v_done, image_of(turn, s, 1))
                pool_ahead((0, 1))
                dve.wait_ge(exp_done, upto(turn, s, NT, NT))
                nc.vector.reciprocal(rowinv[:, :], rowsum[:, :]).then_inc(inv_done, 1)
                dve.wait_ge(inv_done, upto(turn, s, 1, 1))
                for i in range(NT):
                    nc.vector.tensor_scalar(probs[:, i, :], probs[:, i, :], rowinv[:, i:i + 1], None,
                                            ALU.mult).then_inc(p_ready, 1)
                pool_ahead((2,))
                for m in range(MT):
                    dve.wait_ge(pt_hi, upto(turn, s, MT, m + 1))
                    nc.vector.tensor_tensor(pt[LO][:, m, :], t_bank[m][:, :], raw(pt[HI][:, m, :]),
                                            ALU.subtract).then_inc(pt_ready, 1)
                pool_ahead((3,))
                for m in range(DT):
                    dve.wait_ge(att_hi, upto(turn, s, DT, m + 1))
                    nc.vector.scalar_tensor_tensor(out=att[LO][:, m, :], in0=a_bank[m][:, :],
                                                   scalar=bias[:, G_B + m:G_B + m + 1], in1=raw(att[HI][:, m, :]),
                                                   op0=ALU.add, op1=ALU.subtract).then_inc(att_ready, 1)
                if exists(turn, s, 1):
                    lo_q(turn, s + 1)
                    if s % 2:
                        lo_kv(image_of(turn, s, 1))
                for i in range(KT):
                    dve.wait_ge(o_done, upto(turn, s, KT, i + 1))
                    nc.vector.scalar_tensor_tensor(out=xb[s][:, i, :], in0=o_bank[i % 4][:, :],
                                                   scalar=bias[:, Z_B + i:Z_B + i + 1], in1=xb[s][:, i, :],
                                                   op0=ALU.add, op1=ALU.add).then_inc(o_ready, 1)

            steps(dve, step)

        @block.tensor
        def _(pe):
            def product(dst, stationary, moving, start, stop):
                for n, (a, b) in enumerate(PRODUCTS):
                    last = nc.tensor.matmul(dst, stationary(a), moving(b), start=start and n == 0,
                                            stop=stop and n == len(PRODUCTS) - 1)
                return last

            def project_q(turn, s, c):
                pe.wait_ge(x_ready, upto(turn, s, CH, c + 1))
                for m in range(DT):
                    for kt in range(c * KC, (c + 1) * KC):
                        last = product(q_bank[m][:, :], lambda a: theta[a][:, kt, m * P:(m + 1) * P],
                                       lambda b: xs[b][:, kt, :], kt == 0, kt == KT - 1)
                    if c == CH - 1 and m < DT - 1:
                        last.then_inc(q_done, 1)
                return last

            def project_kv(turn, s):
                pe.wait_ge(xp_ready, upto(turn, s, CH, CH))
                for m in range(DT):
                    for kt in range(KT):
                        last = product(k_bank[:, m * M:(m + 1) * M], lambda a: phi[a][:, kt, m * P:(m + 1) * P],
                                       lambda b: xp[b][:, kt, :], kt == 0, kt == KT - 1)
                last.then_inc(k_done, 1)
                for m in range(MT):
                    for kt in range(KT):
                        last = product(v_bank[:, m * D:(m + 1) * D], lambda a: xp[a][:, kt, m * P:(m + 1) * P],
                                       lambda b: gw[b][:, kt, :], kt == 0, kt == KT - 1)
                last.then_inc(v_done, 1)

            pe.wait_ge(w_ready, THETA + 1)
            for c in range(CH):
                project_q(0, 0, c).then_inc(x_used, 1)
            pe.wait_ge(w_ready, len(weights))
            project_kv(0, 1)
            pe.wait_ge(ident_ready, 1)

            def step(turn, s):
                ahead = exists(turn, s, 1)
                pe.wait_ge(k_ready, image_of(turn, s, 1) * DT)
                pe.wait_ge(q_ready, upto(turn, s, DT, DT))
                for i in range(NT):
                    for m in range(DT):
                        last = product(s_bank[i // 2][:, (i % 2) * M:(i % 2 + 1) * M],
                                       lambda a: q[a][:, m, i * P:(i + 1) * P], lambda b: k[b][:, m, :],
                                       m == 0, m == DT - 1)
                    if i % 2:
                        last.then_inc(s_done, 1)
                if ahead:
                    for c in (0, 1):
                        project_q(turn, s + 1, c).then_inc(x_used, 1)
                pe.wait_ge(v_ready, image_of(turn, s, 1))
                for m in range(MT):
                    for i in range(NT):
                        if m == 0:
                            pe.wait_ge(p_ready, upto(turn, s, NT, i + 1))
                        last = nc.tensor.transpose(t_bank[m][:, i * P:(i + 1) * P], probs[:, i, m * P:(m + 1) * P],
                                                   ident[:, :])
                    last.then_inc(t_done, 1)
                if ahead:
                    project_q(turn, s + 1, 2).then_inc(x_used, 1)
                for m in range(DT):
                    for mt in range(MT):
                        if m == 0:
                            pe.wait_ge(pt_ready, upto(turn, s, MT, mt + 1))
                        last = product(a_bank[m][:, :], lambda a: vt[a][:, mt, m * P:(m + 1) * P],
                                       lambda b: pt[b][:, mt, :], mt == 0, mt == MT - 1)
                    last.then_inc(a_done, 1)
                if ahead:
                    project_q(turn, s + 1, 3).then_inc(x_used, 1)
                    if s % 2:
                        project_kv(turn, s + 2)
                pe.wait_ge(att_ready, upto(turn, s, DT, DT))
                for i in range(KT):
                    if i == 2 and s % 2 and ahead:
                        pe.wait_ge(k_ready, image_of(turn, s, 2) * DT)
                    elif i == 3 and s % 2 and ahead:
                        pe.wait_ge(v_ready, image_of(turn, s, 2))
                    elif i >= 4:
                        pe.wait_ge(o_ready, upto(turn, s, KT, i - 3))
                    for m in range(DT):
                        last = product(o_bank[i % 4][:, :], lambda a: zw[a][:, m, i * P:(i + 1) * P],
                                       lambda b: att[b][:, m, :], m == 0, m == DT - 1)
                    last.then_inc(o_done, 1)

            steps(pe, step)


def kernel(x, L0_conv_theta_w, L0_conv_theta_b, L0_conv_phi_w, L0_conv_phi_b, L0_conv_g_w, L0_conv_g_b,
           L0_conv_z_w, L0_conv_z_b):
    import numpy as np
    import concourse.bacc as bacc
    from concourse.bass_utils import run_bass_kernel_spmd

    def columns(b):
        return np.asarray(b).reshape(-1, P).T

    x = np.asarray(x)
    arrays = {
        "x": np.ascontiguousarray(x.reshape(IMAGES, C, N)),
        "theta_wt": np.ascontiguousarray(np.asarray(L0_conv_theta_w).T),
        "phi_wt": np.ascontiguousarray(np.asarray(L0_conv_phi_w).T),
        "g_wt": np.ascontiguousarray(np.asarray(L0_conv_g_w).T),
        "z_wt": np.ascontiguousarray(np.asarray(L0_conv_z_w).T),
        "biases": np.ascontiguousarray(np.concatenate(
            [columns(L0_conv_theta_b), columns(L0_conv_phi_b), columns(L0_conv_g_b), columns(L0_conv_z_b)], axis=1)),
    }
    nc = bacc.Bacc("TRN2", target_bir_lowering=False, num_devices=1, dynamic_dma_scratch_size=1024)
    f32 = mybir.dt.float32
    args = [nc.dram_tensor(name, a.shape, f32, kind="ExternalInput").ap() for name, a in arrays.items()]
    out = nc.dram_tensor("out", (IMAGES, C, N), f32, kind="ExternalOutput").ap()
    non_local_block(nc, *args, out)
    result = run_bass_kernel_spmd(nc, [arrays], core_ids=[0])
    return result.results[0]["out"].reshape(x.shape)
```

```python
import concourse.bass as bass
from concourse import mybir
from contextlib import ExitStack

P = 128
Q = 32
IMAGES = 32
C = 1024
D = 256
SIDE = 32
N = SIDE * SIDE
M = N // 4
KT = C // P
DT = D // P
MT = M // P
H = N // 2
MH = M // 2
NT = H // P
HALVES = 2 * IMAGES
BUFS = 4
TURNS = (HALVES - 1) // BUFS
CH = 4
KC = KT // CH
SCALE = float(D) ** -0.5
STORES = 4
OS = KT // STORES
PIECES = 4
WP = KT * D // PIECES
THETA, PHI, G, Z = range(4)
TH_B, PH_B, G_B, Z_B = 0, DT, 2 * DT, 3 * DT
NB = 3 * DT + KT
HI, LO = 0, 1
PRODUCTS = ((HI, HI), (HI, LO), (LO, HI))


def non_local_block(nc, x, theta_wt, phi_wt, g_wt, z_wt, biases, out):
    f32 = mybir.dt.float32
    f32r = mybir.dt.float32r
    ALU = mybir.AluOpType
    ACT = mybir.ActivationFunctionType
    AX = mybir.AxisListType

    x_v = x.rearrange("(u i) (k p) (j n) -> i j u p k n", i=BUFS // 2, p=P, j=2)
    out_v = out.rearrange("b (k p) (j n) -> b j p k n", p=P, j=2)
    weights_dram = [w.rearrange("(c k p) d -> c p k d", c=PIECES, p=P) for w in (theta_wt, phi_wt, g_wt)]
    z_dram = z_wt.rearrange("(t p) (c n) -> t c p n", p=P, n=WP)

    with ExitStack() as ctx:
        def sb(name, shape, dt):
            return ctx.enter_context(nc.sbuf_tensor(name, shape, dt))

        def sem(name):
            return ctx.enter_context(nc.semaphore(name))

        theta = [sb(f"theta_{s}", [P, KT, D], f32r) for s in ("hi", "lo")]
        phi = [sb(f"phi_{s}", [P, KT, D], f32r) for s in ("hi", "lo")]
        gw = [sb(f"g_{s}", [P, KT, D], f32r) for s in ("hi", "lo")]
        zw = [sb(f"z_{s}", [P, DT, C], f32r) for s in ("hi", "lo")]
        weights = [theta, phi, gw, zw]
        bias = sb("bias", [P, NB], f32)
        phi_bias = sb("phi_bias", [P, DT], f32)
        xb = [sb(f"x{i}", [P, KT, H], f32) for i in range(BUFS)]
        xs = [sb(f"x_split_{s}", [P, KT, H], f32r) for s in ("hi", "lo")]
        rowmax = sb("rowmax", [P, KC * H // 2], f32)
        pooled = sb("pooled", [P, KT, MH], f32)
        xp = [sb(f"xp_{s}", [P, KT, M], f32r) for s in ("hi", "lo")]
        q = [sb(f"q_{s}", [P, DT, H], f32r) for s in ("hi", "lo")]
        k = [sb(f"k_{s}", [P, DT, M], f32r) for s in ("hi", "lo")]
        vt = [sb(f"vt_{s}", [P, MT, D], f32r) for s in ("hi", "lo")]
        probs = sb("probs", [P, NT, M], f32)
        negmax = sb("negmax", [P, NT], f32)
        rowsum = sb("rowsum", [P, NT], f32)
        rowinv = sb("rowinv", [P, NT], f32)
        pt_raw = sb("pt_raw", [P, MT, H], f32)
        pt = [sb(f"pt_{s}", [P, MT, H], f32r) for s in ("hi", "lo")]
        att = [sb(f"att_{s}", [P, DT, H], f32r) for s in ("hi", "lo")]

        bank = [ctx.enter_context(nc.psum_tensor(f"bank{i}", [P, 512], f32)) for i in range(8)]
        q_bank = bank[0:2]
        s_bank = bank[2:4]
        a_bank = bank[4:6]
        o_bank = [bank[6], bank[7], bank[2], bank[3]]
        k_bank, v_bank = bank[6], bank[7]

        w_loaded = [[sem(f"w_loaded{i}{p}") for p in range(PIECES)] for i in range(len(weights))]
        bias_loaded = sem("bias_loaded")
        x_loaded = [[sem(f"x_loaded{i}{c}") for c in range(CH)] for i in range(BUFS)]
        stored = sem("stored")
        w_hi = sem("w_hi")
        w_ready = sem("w_ready")
        phi_bias_ready = sem("phi_bias_ready")
        x_hi = sem("x_hi")
        x_ready = sem("x_ready")
        x_used = sem("x_used")
        rowmax_done = sem("rowmax_done")
        pooled_done = sem("pooled_done")
        xp_hi = sem("xp_hi")
        xp_ready = sem("xp_ready")
        q_done = sem("q_done")
        q_hi = sem("q_hi")
        q_ready = sem("q_ready")
        k_done = sem("k_done")
        k_hi = sem("k_hi")
        k_ready = sem("k_ready")
        v_done = sem("v_done")
        v_hi = sem("v_hi")
        v_ready = sem("v_ready")
        s_done = sem("s_done")
        max_ready = sem("max_ready")
        exp_done = sem("exp_done")
        inv_done = sem("inv_done")
        p_ready = sem("p_ready")
        pt_raw_done = sem("pt_raw_done")
        pt_hi = sem("pt_hi")
        pt_ready = sem("pt_ready")
        a_done = sem("a_done")
        att_hi = sem("att_hi")
        att_ready = sem("att_ready")
        o_done = sem("o_done")
        o_ready = sem("o_ready")

        def raw(t):
            return t.bitcast(f32)

        def flat(t):
            return t[:, :, :].rearrange("p a b -> p (a b)")

        def piece(i, p, part):
            return flat(weights[i][part])[:, p * WP:(p + 1) * WP]

        def staged(i, p):
            at = (i % 2 * PIECES + p) * WP
            return flat(xb[2 + i // 2])[:, at:at + WP]

        def load_weights(eng, i, ps=range(PIECES)):
            for p in ps:
                if i == Z:
                    src, dst = z_dram[p // (PIECES // DT), p % (PIECES // DT)], staged(i, p)
                else:
                    src, dst = weights_dram[i][p], staged(i, p).rearrange("p (k d) -> p k d", d=D)
                eng.dma_start(dst, src).then_inc(w_loaded[i][p], 16)

        def steps(eng, step):
            step(0, 0)
            with eng.Fori(0, TURNS) as turn:
                for s in range(1, BUFS + 1):
                    step(turn, s)
            for s in range(1, BUFS):
                step(TURNS, s)

        def is_first(turn, s):
            return s == 0

        def exists(turn, s, ahead):
            return not isinstance(turn, int) or BUFS * turn + s + ahead < HALVES

        def upto(turn, s, each, more):
            return turn * (BUFS * each) + (s * each + more)

        def image_of(turn, s, more=0):
            return turn * (BUFS // 2) + (s // 2 + more)

        block = ctx.enter_context(nc.Block())

        @block.sync
        def _(sp):
            def load(buf, turn, cs=range(CH)):
                for c in cs:
                    ks = slice(c * KC, (c + 1) * KC)
                    sp.dma_start(xb[buf][:, ks, :], x_v[buf // 2, buf % 2, turn, :, ks, :]).then_inc(x_loaded[buf][c], 16)

            for c in range(CH):
                load_weights(sp, THETA, (c,))
                load(0, 0, (c,))
            load(1, 0)
            for i in (PHI, G, Z):
                load_weights(sp, i)
            sp.wait_ge(w_ready, (PHI + 1) * PIECES)
            load(2, 0)
            sp.wait_ge(w_ready, (Z + 1) * PIECES)
            load(3, 0)

            def store(turn, s):
                for g in range(STORES):
                    sp.wait_ge(o_ready, upto(turn, s, KT, (g + 1) * OS))
                    ks = slice(g * OS, (g + 1) * OS)
                    sp.dma_start(out_v[image_of(turn, s), s % 2, :, ks, :], xb[s % BUFS][:, ks, :]).then_inc(stored, 16)
                if exists(turn, s, BUFS):
                    sp.wait_ge(stored, upto(turn, s, 16 * STORES, 16 * STORES))
                    load(s % BUFS, turn + 1)

            def step(turn, s):
                if not is_first(turn, s):
                    store(turn, s - 1)

            steps(sp, step)
            store(TURNS, BUFS - 1)
            sp.wait_ge(stored, HALVES * STORES * 16)

        @block.scalar
        def _(act):
            act.dma_start(bias[:, :], biases).then_inc(bias_loaded, 16)

            def hi_weights(i, p):
                act.wait_ge(w_loaded[i][p], 16)
                nc.scalar.activation(piece(i, p, HI), staged(i, p), ACT.Copy,
                                     scale=SCALE if i == PHI else 1.0).then_inc(w_hi, 1)

            def hi_x(turn, s, c):
                ks = slice(c * KC, (c + 1) * KC)
                act.wait_ge(x_loaded[s % BUFS][c], turn * 16 + 16 * (s // BUFS + 1))
                nc.scalar.activation(xs[HI][:, ks, :], xb[s % BUFS][:, ks, :], ACT.Copy).then_inc(x_hi, 1)

            def hi_pooled(turn, s):
                act.wait_ge(pooled_done, upto(turn, s, CH, CH))
                nc.scalar.activation(xp[HI][:, :, (s % 2) * MH:(s % 2 + 1) * MH], pooled[:, :, :], ACT.Copy).then_inc(xp_hi, 1)

            def hi_q(turn, s):
                for m in range(DT):
                    if m < DT - 1:
                        act.wait_ge(q_done, upto(turn, s, DT - 1, m + 1))
                    else:
                        act.wait_ge(x_used, upto(turn, s, CH, CH))
                    nc.scalar.activation(q[HI][:, m, :], q_bank[m][:, :], ACT.Identity,
                                         bias=bias[:, TH_B + m:TH_B + m + 1]).then_inc(q_hi, 1)

            def hi_k(image):
                act.wait_ge(k_done, image + 1)
                for m in range(DT):
                    nc.scalar.activation(k[HI][:, m, :], k_bank[:, m * M:(m + 1) * M], ACT.Identity,
                                         bias=phi_bias[:, m:m + 1]).then_inc(k_hi, 1)

            def hi_att(turn, s):
                for m in range(DT):
                    act.wait_ge(a_done, upto(turn, s, DT, m + 1))
                    nc.scalar.activation(att[HI][:, m, :], a_bank[m][:, :], ACT.Identity,
                                         bias=bias[:, G_B + m:G_B + m + 1]).then_inc(att_hi, 1)

            for c in range(CH):
                hi_weights(THETA, c)
                hi_x(0, 0, c)
            hi_pooled(0, 0)
            for p in range(PIECES):
                hi_weights(PHI, p)
            hi_pooled(0, 1)
            act.wait_ge(bias_loaded, 16)
            hi_q(0, 0)
            for p in range(PIECES):
                hi_weights(G, p)
            for c in range(CH):
                act.wait_ge(x_used, c + 1)
                hi_x(0, 1, c)
            for p in range(PIECES):
                hi_weights(Z, p)
            act.wait_ge(phi_bias_ready, 1)
            hi_k(0)

            def step(turn, s):
                def hi_x_ahead(c):
                    if exists(turn, s, 2):
                        act.wait_ge(x_used, upto(turn, s + 1, CH, c + 1))
                        hi_x(turn, s + 2, c)

                if not is_first(turn, s):
                    hi_att(turn, s - 1)
                if s % 2 == 0:
                    act.wait_ge(v_done, image_of(turn, s, 1))
                    nc.scalar.activation(flat(vt[HI]), v_bank[:, :], ACT.Copy).then_inc(v_hi, 1)
                for i in range(NT):
                    if i % 2 == 0:
                        act.wait_ge(max_ready, upto(turn, s, 2, i // 2 + 1))
                    nc.scalar.activation(probs[:, i, :], s_bank[i // 2][:, (i % 2) * M:(i % 2 + 1) * M], ACT.Exp,
                                         bias=negmax[:, i:i + 1], accum_out=rowsum[:, i:i + 1]).then_inc(exp_done, 1)
                act.wait_ge(inv_done, upto(turn, s, 1, 1))
                for i in range(NT):
                    nc.scalar.activation(probs[:, i, :], probs[:, i, :], ACT.Copy, scale=rowinv[:, i:i + 1]).then_inc(p_ready, 1)
                for c in (0, 1, 2):
                    hi_x_ahead(c)
                if exists(turn, s, 1):
                    hi_q(turn, s + 1)
                act.wait_ge(pt_raw_done, upto(turn, s, P // Q, P // Q))
                nc.scalar.activation(flat(pt[HI]), flat(pt_raw), ACT.Copy).then_inc(pt_hi, 1)
                if exists(turn, s, 2):
                    hi_pooled(turn, s + 2)
                hi_x_ahead(3)
                if s % 2 and exists(turn, s, 1):
                    hi_k(image_of(turn, s, 1))

            steps(act, step)
            hi_att(TURNS, BUFS - 1)

        @block.gpsimd
        def _(pool):
            def lo_x(turn, s, c):
                ks = slice(c * KC, (c + 1) * KC)
                pool.wait_ge(x_hi, upto(turn, s, CH, c + 1))
                nc.gpsimd.tensor_tensor(xs[LO][:, ks, :], xb[s % BUFS][:, ks, :], raw(xs[HI][:, ks, :]),
                                        ALU.subtract).then_inc(x_ready, 1)

            for h in range(2):
                for c in range(CH):
                    lo_x(0, h, c)

            def step(turn, s):
                ahead = exists(turn, s, 2)
                for c in (0, 1, 2) if ahead else ():
                    lo_x(turn, s + 2, c)
                pool.wait_ge(pt_hi, upto(turn, s, 1, 1))
                nc.gpsimd.tensor_tensor(flat(pt[LO]), flat(pt_raw), raw(flat(pt[HI])), ALU.subtract).then_inc(pt_ready, 1)
                if ahead:
                    ms = slice((s % 2) * MH, (s % 2 + 1) * MH)
                    pool.wait_ge(xp_hi, upto(turn, s + 2, 1, 1))
                    nc.gpsimd.tensor_tensor(xp[LO][:, :, ms], pooled[:, :, :], raw(xp[HI][:, :, ms]),
                                            ALU.subtract).then_inc(xp_ready, 1)
                    lo_x(turn, s + 2, 3)

            steps(pool, step)

        @block.vector
        def _(dve):
            def lo_weights(i, p):
                dve.wait_ge(w_hi, i * PIECES + p + 1)
                nc.vector.scalar_tensor_tensor(out=piece(i, p, LO), in0=staged(i, p),
                                               scalar=SCALE if i == PHI else 1.0, in1=raw(piece(i, p, HI)),
                                               op0=ALU.mult, op1=ALU.subtract).then_inc(w_ready, 1)

            def max_pool(turn, s, c):
                ks = slice(c * KC, (c + 1) * KC)
                dve.wait_ge(x_loaded[s % BUFS][c], turn * 16 + 16 * (s // BUFS + 1))
                if not (is_first(turn, s) and c == 0):
                    dve.wait_ge(pooled_done, upto(turn, s, CH, c))
                rows = xb[s % BUFS][:, ks, :].rearrange("p k (r two w) -> p (k r) two w", two=2, w=SIDE)
                nc.vector.tensor_tensor(rowmax[:, :].rearrange("p (r w) -> p r w", w=SIDE), rows[:, :, 0, :],
                                        rows[:, :, 1, :], ALU.max).then_inc(rowmax_done, 1)
                dve.wait_ge(rowmax_done, upto(turn, s, CH, c + 1))
                cols = rowmax[:, :].rearrange("p (w two) -> p w two", two=2)
                nc.vector.tensor_tensor(flat(pooled)[:, c * KC * MH:(c + 1) * KC * MH], cols[:, :, 0], cols[:, :, 1],
                                        ALU.max).then_inc(pooled_done, 1)

            def lo_q(turn, s):
                for m in range(DT):
                    dve.wait_ge(q_hi, upto(turn, s, DT, m + 1))
                    nc.vector.scalar_tensor_tensor(out=q[LO][:, m, :], in0=q_bank[m][:, :],
                                                   scalar=bias[:, TH_B + m:TH_B + m + 1], in1=raw(q[HI][:, m, :]),
                                                   op0=ALU.add, op1=ALU.subtract).then_inc(q_ready, 1)

            def lo_k(image):
                dve.wait_ge(k_hi, image * DT + DT)
                for m in range(DT):
                    nc.vector.scalar_tensor_tensor(out=k[LO][:, m, :], in0=k_bank[:, m * M:(m + 1) * M],
                                                   scalar=phi_bias[:, m:m + 1], in1=raw(k[HI][:, m, :]),
                                                   op0=ALU.add, op1=ALU.subtract).then_inc(k_ready, 1)

            def lo_att(turn, s):
                for m in range(DT):
                    dve.wait_ge(att_hi, upto(turn, s, DT, m + 1))
                    nc.vector.scalar_tensor_tensor(out=att[LO][:, m, :], in0=a_bank[m][:, :],
                                                   scalar=bias[:, G_B + m:G_B + m + 1], in1=raw(att[HI][:, m, :]),
                                                   op0=ALU.add, op1=ALU.subtract).then_inc(att_ready, 1)

            def transpose_probs(b):
                for a in range(P // Q):
                    src = probs[a * Q:(a + 1) * Q, :, :].rearrange("p i (t b m) -> p i t b m", t=MT, m=Q)[:, :, :, b, :]
                    dst = pt_raw[b * Q:(b + 1) * Q, :, :].rearrange("p t (i a n) -> p i t a n", i=NT, n=Q)[:, :, :, a, :]
                    last = nc.vector.transpose(dst, src)
                last.then_inc(pt_raw_done, 1)

            def finish(turn, s, tiles):
                for i in tiles:
                    dve.wait_ge(o_done, upto(turn, s, KT, i + 1))
                    tile = xb[s % BUFS][:, i, :]
                    nc.vector.scalar_tensor_tensor(out=tile, in0=o_bank[i % 4][:, :], scalar=bias[:, Z_B + i:Z_B + i + 1],
                                                   in1=tile, op0=ALU.add, op1=ALU.add).then_inc(o_ready, 1)

            for c in range(CH):
                lo_weights(THETA, c)
                max_pool(0, 0, c)
            for h in range(2):
                if h == 1:
                    for c in range(CH):
                        max_pool(0, 1, c)
                    for p in range(PIECES):
                        lo_weights(PHI, p)
                ms = slice(h * MH, (h + 1) * MH)
                dve.wait_ge(xp_hi, h + 1)
                nc.vector.tensor_tensor(xp[LO][:, :, ms], pooled[:, :, :], raw(xp[HI][:, :, ms]),
                                        ALU.subtract).then_inc(xp_ready, 1)
            dve.wait_ge(bias_loaded, 16)
            nc.vector.tensor_scalar(phi_bias[:, :], bias[:, PH_B:PH_B + DT], SCALE, None,
                                    ALU.mult).then_inc(phi_bias_ready, 1)
            lo_q(0, 0)
            for i in (G, Z):
                for p in range(PIECES):
                    lo_weights(i, p)
            dve.wait_ge(phi_bias_ready, 1)
            lo_k(0)

            def step(turn, s):
                def pool_ahead(c):
                    if exists(turn, s, 2):
                        max_pool(turn, s + 2, c)

                if not is_first(turn, s):
                    lo_att(turn, s - 1)
                if s % 2 == 0:
                    dve.wait_ge(v_hi, image_of(turn, s, 1))
                    nc.vector.tensor_tensor(flat(vt[LO]), v_bank[:, :], raw(flat(vt[HI])), ALU.subtract).then_inc(v_ready, 1)
                for b in range(2):
                    dve.wait_ge(s_done, upto(turn, s, 2, b + 1))
                    nc.vector.tensor_reduce(negmax[:, 2 * b:2 * b + 2], s_bank[b][:, :].rearrange("p (i m) -> p i m", m=M),
                                            AX.X, ALU.max, negate=True).then_inc(max_ready, 1)
                dve.wait_ge(exp_done, upto(turn, s, NT, NT))
                nc.vector.reciprocal(rowinv[:, :], rowsum[:, :]).then_inc(inv_done, 1)
                if exists(turn, s, 2):
                    dve.wait_ge(xp_ready, upto(turn, s + 1, 1, 1))
                pool_ahead(0)
                if not exists(turn, s, 1):
                    finish(turn, s - 1, (0, 1))
                    dve.wait_ge(p_ready, upto(turn, s, NT, NT))
                    for b, tiles in enumerate(((), (), (2,), (3, 4, 5, 6, 7))):
                        transpose_probs(b)
                        finish(turn, s - 1, tiles)
                    return
                dve.wait_ge(p_ready, upto(turn, s, NT, NT))
                for b in range(P // Q):
                    transpose_probs(b)
                pool_ahead(1)
                pool_ahead(2)
                lo_q(turn, s + 1)
                pool_ahead(3)
                if not is_first(turn, s):
                    finish(turn, s - 1, range(KT))
                if s % 2:
                    lo_k(image_of(turn, s, 1))

            steps(dve, step)
            lo_att(TURNS, BUFS - 1)
            finish(TURNS, BUFS - 1, range(KT))

        @block.tensor
        def _(pe):
            def product(dst, stationary, moving, start, stop):
                for n, (a, b) in enumerate(PRODUCTS):
                    last = nc.tensor.matmul(dst, stationary(a), moving(b), start=start and n == 0,
                                            stop=stop and n == len(PRODUCTS) - 1)
                return last

            def project_q(turn, s, c):
                pe.wait_ge(x_ready, upto(turn, s, CH, c + 1))
                for m in range(DT):
                    for kt in range(c * KC, (c + 1) * KC):
                        last = product(q_bank[m][:, :], lambda a: theta[a][:, kt, m * P:(m + 1) * P],
                                       lambda b: xs[b][:, kt, :], kt == 0, kt == KT - 1)
                    if c == CH - 1 and m < DT - 1:
                        last.then_inc(q_done, 1)
                last.then_inc(x_used, 1)

            def project_k():
                for m in range(DT):
                    for kt in range(KT):
                        last = product(k_bank[:, m * M:(m + 1) * M], lambda a: phi[a][:, kt, m * P:(m + 1) * P],
                                       lambda b: xp[b][:, kt, :], kt == 0, kt == KT - 1)
                last.then_inc(k_done, 1)

            def project_v():
                for m in range(MT):
                    for kt in range(KT):
                        last = product(v_bank[:, m * D:(m + 1) * D], lambda a: xp[a][:, kt, m * P:(m + 1) * P],
                                       lambda b: gw[b][:, kt, :], kt == 0, kt == KT - 1)
                last.then_inc(v_done, 1)

            def project_out(turn, s, banks_free):
                pe.wait_ge(att_ready, upto(turn, s, DT, DT))
                for i in range(KT):
                    if i == 2 and not banks_free:
                        pe.wait_ge(exp_done, upto(turn, s + 1, NT, NT))
                    if i >= 4:
                        pe.wait_ge(o_ready, upto(turn, s, KT, i - 3))
                    for m in range(DT):
                        last = product(o_bank[i % 4][:, :], lambda a: zw[a][:, m, i * P:(i + 1) * P],
                                       lambda b: att[b][:, m, :], m == 0, m == DT - 1)
                    last.then_inc(o_done, 1)

            for c in range(CH):
                pe.wait_ge(w_ready, THETA * PIECES + c + 1)
                project_q(0, 0, c)
            pe.wait_ge(w_ready, (PHI + 1) * PIECES)
            pe.wait_ge(xp_ready, 2)
            project_k()
            pe.wait_ge(w_ready, (G + 1) * PIECES)
            project_v()
            pe.wait_ge(w_ready, (Z + 1) * PIECES)

            def step(turn, s):
                pe.wait_ge(k_ready, image_of(turn, s, 1) * DT)
                pe.wait_ge(q_ready, upto(turn, s, DT, DT))
                for i in range(NT):
                    for m in range(DT):
                        last = product(s_bank[i // 2][:, (i % 2) * M:(i % 2 + 1) * M],
                                       lambda a: q[a][:, m, i * P:(i + 1) * P], lambda b: k[b][:, m, :],
                                       m == 0, m == DT - 1)
                    if i % 2:
                        last.then_inc(s_done, 1)
                if exists(turn, s, 1):
                    for c in range(CH):
                        project_q(turn, s + 1, c)
                pe.wait_ge(v_ready, image_of(turn, s, 1))
                if not is_first(turn, s):
                    project_out(turn, s - 1, False)
                ahead = s % 2 and exists(turn, s, 1)
                if ahead:
                    pe.wait_ge(xp_ready, upto(turn, s + 2, 1, 1))
                    pe.wait_ge(o_ready, upto(turn, s - 1, KT, 5))
                    project_k()
                pe.wait_ge(pt_ready, upto(turn, s, 1, 1))
                for m in range(DT):
                    for mt in range(MT):
                        last = product(a_bank[m][:, :], lambda a: vt[a][:, mt, m * P:(m + 1) * P],
                                       lambda b: pt[b][:, mt, :], mt == 0, mt == MT - 1)
                    last.then_inc(a_done, 1)
                if ahead:
                    pe.wait_ge(o_ready, upto(turn, s - 1, KT, 6))
                    project_v()
                if not is_first(turn, s):
                    pe.wait_ge(o_ready, upto(turn, s - 1, KT, KT))

            steps(pe, step)
            project_out(TURNS, BUFS - 1, True)


def kernel(x, L0_conv_theta_w, L0_conv_theta_b, L0_conv_phi_w, L0_conv_phi_b, L0_conv_g_w, L0_conv_g_b,
           L0_conv_z_w, L0_conv_z_b):
    import numpy as np
    import concourse.bacc as bacc
    from concourse.bass_utils import run_bass_kernel_spmd

    def columns(b):
        return np.asarray(b).reshape(-1, P).T

    x = np.asarray(x)
    arrays = {
        "x": np.ascontiguousarray(x.reshape(IMAGES, C, N)),
        "theta_wt": np.ascontiguousarray(np.asarray(L0_conv_theta_w).T),
        "phi_wt": np.ascontiguousarray(np.asarray(L0_conv_phi_w).T),
        "g_wt": np.ascontiguousarray(np.asarray(L0_conv_g_w).T),
        "z_wt": np.ascontiguousarray(np.asarray(L0_conv_z_w).T),
        "biases": np.ascontiguousarray(np.concatenate(
            [columns(L0_conv_theta_b), columns(L0_conv_phi_b), columns(L0_conv_g_b), columns(L0_conv_z_b)], axis=1)),
    }
    nc = bacc.Bacc("TRN2", target_bir_lowering=False, num_devices=1, dynamic_dma_scratch_size=1024)
    f32 = mybir.dt.float32
    args = [nc.dram_tensor(name, a.shape, f32, kind="ExternalInput").ap() for name, a in arrays.items()]
    out = nc.dram_tensor("out", (IMAGES, C, N), f32, kind="ExternalOutput").ap()
    non_local_block(nc, *args, out)
    result = run_bass_kernel_spmd(nc, [arrays], core_ids=[0])
    return result.results[0]["out"].reshape(x.shape)
```
